# Optimizing a Trainium2 kernel written in Bass

```python
import numpy as np
import jax
import jax.numpy as jnp

def _softmax(x, axis=-1):
    return jax.nn.softmax(x, axis=axis)

def _gelu(x):
    return jax.nn.gelu(x, approximate=True)

def _silu(x):
    return jax.nn.silu(x)

def _sigmoid(x):
    return jax.nn.sigmoid(x)

def _layernorm(x, axis=-1, eps=1e-05):
    m = jnp.mean(x, axis=axis, keepdims=True)
    v = jnp.var(x, axis=axis, keepdims=True)
    return (x - m) / jnp.sqrt(v + eps)

def _scatter_add(tgt, idx, src, axis=0):
    return tgt.at[idx].add(src)

def _segment_sum(src, seg, n):
    return jax.ops.segment_sum(src, seg, n)
kernel_name = 'mk_decoder_postln_d1_seqx_r4_cb35d7'

def setup_inputs(seed: int=0):
    np.random.seed(seed)
    _w = jnp.asarray

    def _rec_inputs():
        import jax
        import jax.numpy as jnp
        _rk = jax.random.key(seed)
        x = -9.806e-05 + 1 * jax.random.normal(jax.random.fold_in(_rk, 1), (4, 1024, 256), jnp.float32)
        _lenS = 1024 - jax.random.randint(jax.random.fold_in(_rk, 7), (4,), 0, max(1, 1024 // 4) + 1, jnp.int32)
        _lenS2 = 64 - jax.random.randint(jax.random.fold_in(_rk, 8), (4,), 0, max(1, 64 // 4) + 1, jnp.int32)
        _ctx_1024P = jax.random.normal(jax.random.fold_in(_rk, 11), (4, 16, 256), jnp.float32)
        _ctx_1024c = jax.random.dirichlet(jax.random.fold_in(_rk, 511), 0.3 * jnp.ones((16,), jnp.float32), (4, 64))
        _ctx_1024t = jnp.einsum('bsk,bkd->bsd', _ctx_1024c, _ctx_1024P)
        _ctx_1024t = _ctx_1024t * jax.lax.rsqrt(jnp.mean(jnp.square(_ctx_1024t)) + 1e-12) * 0.953939
        ctx_1024 = -1.52775e-05 + 0.999936 * (_ctx_1024t + 0.3 * jax.random.normal(jax.random.fold_in(_rk, 611), (4, 64, 256), jnp.float32))
        return (x, ctx_1024)
    x, ctx_1024 = _rec_inputs()

    def _L0_attn_setup():
        import jax, jax.numpy as jnp
        import numpy as np
        LN_EPS = 1e-05

        def _forward(x, W_in, conv_w, conv_b, a_param, W_out, ln_w, ln_b):
            B, T, D = x.shape
            K = conv_w.shape[-1]
            proj = jnp.einsum('btd,ed->bte', x, W_in)
            gate, val = (proj[..., :D], proj[..., D:])
            g = jax.nn.sigmoid(gate)
            v = jax.lax.conv_general_dilated(val.transpose(0, 2, 1), conv_w, window_strides=(1,), padding=[(K // 2, K // 2)], feature_group_count=D, dimension_numbers=('NCH', 'OIH', 'NCH'))
            v = (v + conv_b[None, :, None]).transpose(0, 2, 1)
            a = jnp.tanh(a_param)
            gv = g * v

            def step(h, u):
                h = a * h + u
                return (h, h)
            h0 = jnp.zeros((B, D), dtype=x.dtype)
            _, y = jax.lax.scan(step, h0, gv.transpose(1, 0, 2))
            y = y.transpose(1, 0, 2)
            res = x + jnp.einsum('btd,ed->bte', y, W_out)
            mu = jnp.mean(res, axis=-1, keepdims=True)
            var = jnp.mean(jnp.square(res - mu), axis=-1, keepdims=True)
            return (res - mu) * jax.lax.rsqrt(var + LN_EPS) * ln_w + ln_b
        key = jax.random.key(seed)
        ks = jax.random.split(key, 6)
        B, T, D, K = (8, 512, 256, 5)
        x = jax.random.normal(ks[0], (B, T, D), dtype=jnp.float32)
        W_in = jax.random.normal(ks[1], (2 * D, D), dtype=jnp.float32) * (1.0 / np.sqrt(D))
        conv_w = jax.random.normal(ks[2], (D, 1, K), dtype=jnp.float32) * (1.0 / np.sqrt(K))
        conv_b = jax.random.normal(ks[3], (D,), dtype=jnp.float32) * 0.1
        a_param = jax.random.normal(ks[4], (D,), dtype=jnp.float32)
        W_out = jax.random.normal(ks[5], (D, D), dtype=jnp.float32) * (1.0 / np.sqrt(D))
        ln_w = jnp.ones((D,), dtype=jnp.float32)
        ln_b = jnp.zeros((D,), dtype=jnp.float32)
        return {'x': x, 'W_in': W_in, 'conv_w': conv_w, 'conv_b': conv_b, 'a_param': a_param, 'W_out': W_out, 'ln_w': ln_w, 'ln_b': ln_b}
    _L0_attn_all = _L0_attn_setup()
    _L0_attn_in = {k: v for k, v in _L0_attn_all.items() if k in ('W_in', 'conv_w', 'conv_b', 'a_param', 'W_out', 'ln_w', 'ln_b')}
    del _L0_attn_all

    def _L0_xattn_setup():
        import jax, jax.numpy as jnp
        import numpy as np
        D = 256
        NUM_ITERS = 3
        EPS = 1e-06
        SCALE = D ** (-0.5)

        def rmsnorm(x, w, eps=EPS):
            return x * jax.lax.rsqrt(jnp.mean(x * x, axis=-1, keepdims=True) + eps) * w

        def gru_cell(x, h, wih, whh, bih, bhh):
            gx = x @ wih.T + bih
            gh = h @ whh.T + bhh
            xr, xz, xn = jnp.split(gx, 3, axis=-1)
            hr, hz, hn = jnp.split(gh, 3, axis=-1)
            r = jax.nn.sigmoid(xr + hr)
            z = jax.nn.sigmoid(xz + hz)
            n = jnp.tanh(xn + r * hn)
            return (1.0 - z) * n + z * h
        key = jax.random.key(seed)
        ks = jax.random.split(key, 8)
        B, K, M, d = (8, 64, 1024, D)
        w_std = d ** (-0.5)
        return {'slots': jax.random.normal(ks[0], (B, K, d), jnp.float32), 'P': jax.random.normal(ks[1], (B, M, d), jnp.float32), 'Wq': jax.random.normal(ks[2], (d, d), jnp.float32) * w_std, 'Wk': jax.random.normal(ks[3], (d, d), jnp.float32) * w_std, 'Wv': jax.random.normal(ks[4], (d, d), jnp.float32) * w_std, 'gru_wih': jax.random.normal(ks[5], (3 * d, d), jnp.float32) * w_std, 'gru_whh': jax.random.normal(ks[6], (3 * d, d), jnp.float32) * w_std, 'gru_bih': jnp.zeros((3 * d,), jnp.float32), 'gru_bhh': jnp.zeros((3 * d,), jnp.float32), 'slot_norm_w': jnp.ones((d,), jnp.float32), 'input_norm_w': jnp.ones((d,), jnp.float32)}
    _L0_xattn_all = _L0_xattn_setup()
    _L0_xattn_in = {k: v for k, v in _L0_xattn_all.items() if k in ('Wq', 'Wk', 'Wv', 'gru_wih', 'gru_whh', 'gru_bih', 'gru_bhh', 'slot_norm_w', 'input_norm_w')}
    del _L0_xattn_all

    def _L0_ffn_setup():
        import jax, jax.numpy as jnp
        import numpy as np
        B, S, H, E = (2, 2048, 256, 8)
        SCALE = 0.5
        key = jax.random.key(seed)
        k1, k2 = jax.random.split(key)
        x = jax.random.normal(k1, (B, S, H), dtype=jnp.float32)
        gate_w = jax.random.normal(k2, (E, H), dtype=jnp.float32) * 0.02
        coeff = SCALE * (1.0 + 0.05 * jnp.arange(E, dtype=jnp.float32))
        expert_w = coeff[:, None, None] * jnp.eye(H, dtype=jnp.float32)
        return {'x': x, 'gate_w': gate_w, 'expert_w': expert_w}
    _L0_ffn_all = _L0_ffn_setup()
    _L0_ffn_in = {k: v for k, v in _L0_ffn_all.items() if k in ('gate_w', 'expert_w')}
    del _L0_ffn_all
    return {'x': x, 'ctx_1024': ctx_1024, 'L0_attn_W_in': _L0_attn_in['W_in'], 'L0_attn_conv_w': _L0_attn_in['conv_w'], 'L0_attn_conv_b': _L0_attn_in['conv_b'], 'L0_attn_a_param': _L0_attn_in['a_param'], 'L0_attn_W_out': _L0_attn_in['W_out'], 'L0_attn_ln_w': _L0_attn_in['ln_w'], 'L0_attn_ln_b': _L0_attn_in['ln_b'], 'L0_xattn_Wq': _L0_xattn_in['Wq'], 'L0_xattn_Wk': _L0_xattn_in['Wk'], 'L0_xattn_Wv': _L0_xattn_in['Wv'], 'L0_xattn_gru_wih': _L0_xattn_in['gru_wih'], 'L0_xattn_gru_whh': _L0_xattn_in['gru_whh'], 'L0_xattn_gru_bih': _L0_xattn_in['gru_bih'], 'L0_xattn_gru_bhh': _L0_xattn_in['gru_bhh'], 'L0_xattn_slot_norm_w': _L0_xattn_in['slot_norm_w'], 'L0_xattn_input_norm_w': _L0_xattn_in['input_norm_w'], 'L0_ffn_gate_w': _L0_ffn_in['gate_w'], 'L0_ffn_expert_w': _L0_ffn_in['expert_w']}

def reference(x, ctx_1024, L0_attn_W_in, L0_attn_conv_w, L0_attn_conv_b, L0_attn_a_param, L0_attn_W_out, L0_attn_ln_w, L0_attn_ln_b, L0_xattn_Wq, L0_xattn_Wk, L0_xattn_Wv, L0_xattn_gru_wih, L0_xattn_gru_whh, L0_xattn_gru_bih, L0_xattn_gru_bhh, L0_xattn_slot_norm_w, L0_xattn_input_norm_w, L0_ffn_gate_w, L0_ffn_expert_w):
    import jax
    import jax.numpy as jnp

    def _L0_attn_ref(x, W_in, conv_w, conv_b, a_param, W_out, ln_w, ln_b):
        import jax, jax.numpy as jnp
        import numpy as np
        LN_EPS = 1e-05

        def _forward(x, W_in, conv_w, conv_b, a_param, W_out, ln_w, ln_b):
            B, T, D = x.shape
            K = conv_w.shape[-1]
            proj = jnp.einsum('btd,ed->bte', x, W_in)
            gate, val = (proj[..., :D], proj[..., D:])
            g = jax.nn.sigmoid(gate)
            v = jax.lax.conv_general_dilated(val.transpose(0, 2, 1), conv_w, window_strides=(1,), padding=[(K // 2, K // 2)], feature_group_count=D, dimension_numbers=('NCH', 'OIH', 'NCH'))
            v = (v + conv_b[None, :, None]).transpose(0, 2, 1)
            a = jnp.tanh(a_param)
            gv = g * v

            def step(h, u):
                h = a * h + u
                return (h, h)
            h0 = jnp.zeros((B, D), dtype=x.dtype)
            _, y = jax.lax.scan(step, h0, gv.transpose(1, 0, 2))
            y = y.transpose(1, 0, 2)
            res = x + jnp.einsum('btd,ed->bte', y, W_out)
            mu = jnp.mean(res, axis=-1, keepdims=True)
            var = jnp.mean(jnp.square(res - mu), axis=-1, keepdims=True)
            return (res - mu) * jax.lax.rsqrt(var + LN_EPS) * ln_w + ln_b
        return _forward(x, W_in, conv_w, conv_b, a_param, W_out, ln_w, ln_b)

    def _L0_xattn_ref(slots, P, Wq, Wk, Wv, gru_wih, gru_whh, gru_bih, gru_bhh, slot_norm_w, input_norm_w):
        import jax, jax.numpy as jnp
        import numpy as np
        D = 256
        NUM_ITERS = 3
        EPS = 1e-06
        SCALE = D ** (-0.5)

        def rmsnorm(x, w, eps=EPS):
            return x * jax.lax.rsqrt(jnp.mean(x * x, axis=-1, keepdims=True) + eps) * w

        def gru_cell(x, h, wih, whh, bih, bhh):
            gx = x @ wih.T + bih
            gh = h @ whh.T + bhh
            xr, xz, xn = jnp.split(gx, 3, axis=-1)
            hr, hz, hn = jnp.split(gh, 3, axis=-1)
            r = jax.nn.sigmoid(xr + hr)
            z = jax.nn.sigmoid(xz + hz)
            n = jnp.tanh(xn + r * hn)
            return (1.0 - z) * n + z * h
        Pn = rmsnorm(P, input_norm_w)
        k_proj = Pn @ Wk.T
        v_proj = Pn @ Wv.T
        for _ in range(NUM_ITERS):
            sn = rmsnorm(slots, slot_norm_w)
            q_proj = sn @ Wq.T
            scores = jnp.einsum('bkd,bmd->bkm', q_proj, k_proj) * SCALE
            attn = jax.nn.softmax(scores, axis=-2)
            attn = attn / (jnp.sum(attn, axis=-1, keepdims=True) + EPS)
            updates = jnp.einsum('bkm,bmd->bkd', attn, v_proj)
            slots = gru_cell(updates, slots, gru_wih, gru_whh, gru_bih, gru_bhh)
        return slots

    def _L0_ffn_ref(x, gate_w, expert_w):
        import jax, jax.numpy as jnp
        import numpy as np
        B, S, H, E = (2, 2048, 256, 8)
        SCALE = 0.5
        scores = jnp.einsum('bsh,eh->bse', x, gate_w)
        chosen = jnp.argmax(scores, axis=-1)
        onehot = jax.nn.one_hot(chosen, gate_w.shape[0], dtype=x.dtype)
        expert_out = jnp.einsum('bsh,efh->bsef', x, expert_w)
        return x + jnp.einsum('bsef,bse->bsf', expert_out, onehot)
    x = _layernorm(x + _L0_attn_ref(x, L0_attn_W_in, L0_attn_conv_w, L0_attn_conv_b, L0_attn_a_param, L0_attn_W_out, L0_attn_ln_w, L0_attn_ln_b), axis=-1)
    x = _layernorm(x + _L0_xattn_ref(x, ctx_1024, L0_xattn_Wq, L0_xattn_Wk, L0_xattn_Wv, L0_xattn_gru_wih, L0_xattn_gru_whh, L0_xattn_gru_bih, L0_xattn_gru_bhh, L0_xattn_slot_norm_w, L0_xattn_input_norm_w), axis=-1)
    x = _layernorm(x + _L0_ffn_ref(x, L0_ffn_gate_w, L0_ffn_expert_w), axis=-1)
    return x

_drawn_inputs = setup_inputs


def setup_inputs(seed=0):
    import zlib

    import numpy as np

    out = dict(_drawn_inputs(seed))
    spreads = {'L0_attn_ln_w': (1.0, 0.2),
     'L0_attn_ln_b': (0.0, 0.1),
     'L0_xattn_gru_bih': (0.0, 0.1),
     'L0_xattn_gru_bhh': (0.0, 0.1),
     'L0_xattn_slot_norm_w': (1.0, 0.6),
     'L0_xattn_input_norm_w': (1.0, 0.2)}
    factors = {'L0_ffn_gate_w': 8.0}
    for name, (base, spread) in spreads.items():
        noise = np.random.default_rng([zlib.crc32(name.encode()), seed]).standard_normal(out[name].shape)
        drawn = base * np.exp(spread * noise) if base else spread * noise
        out[name] = jnp.asarray(drawn.astype(out[name].dtype))
    for name, factor in factors.items():
        out[name] = (out[name] * factor).astype(out[name].dtype)
    return out
```

```python
from contextlib import ExitStack

import concourse.bass as bass
from concourse import mybir

ALU = mybir.AluOpType
ACT = mybir.ActivationFunctionType
F32 = mybir.dt.float32
F32R = mybir.dt.float32r
I32 = mybir.dt.int32
AX_X = mybir.AxisListType.X

P = 128
BANK = 512
EPS_LN = 1e-5
EPS_RMS = 1e-6
EPS_ATTN = 1e-6
B = 4
ITERS = 3
RSQRT_SEED = 0x5F3759DF
PASSES = ((0, 0), (1, 0), (0, 1))


def decoder_layer(nc, x, xT, ctxT, vecs, w_inT, w_outT, wq, wkT, wvT, wihT, whhT, gateT, expertT,
                  lnw, lnb, ident_in, order_in, out, x1_dram):
    TOK, D = x.shape
    M = ctxT.shape[1] // B
    T = TOK // B
    C = D // P
    J = T // BANK
    TJ = BANK // P
    NT = T // P
    G3 = wihT.shape[1]
    E = gateT.shape[1]
    K = 5
    HALO = K // 2
    V_CB, V_A, V_SN, V_IN, V_BIH, V_BHH = K, K + 1, K + 2, K + 3, K + 4, K + 7
    NV = K + 10
    STEPS = ITERS * B
    U = J * C
    SCALE = float(D) ** -0.5
    assert C == 2 and J == 2 and TJ == 4 and 2 * M == P and vecs.shape[2] == NV

    x_v = x.rearrange("(b t p) d -> p b t d", b=B, p=P)
    x1_v = x1_dram.rearrange("(b t p) d -> p b t d", b=B, p=P)
    out_v = out.rearrange("(b t p) d -> p b t d", b=B, p=P)
    xT_v = xT.rearrange("(c p) (b t) -> p c b t", p=P, b=B)

    def chunks(w):
        return w.rearrange("(c p) n -> p c n", p=P)

    root = ExitStack()
    with root:
        def space(stack):
            def sb(name, shape, dt=F32):
                return stack.enter_context(nc.sbuf_tensor(name, shape, dt))
            return sb

        def sem(name):
            return root.enter_context(nc.semaphore(name))

        sb = space(root)
        psum = root.enter_context(nc.psum_tensor("psum", [P, 8, BANK], F32))

        slots = [sb("slots_hi", [P, C, B, T], F32R), sb("slots_lo", [P, C, B, T], F32R)]
        rstd = sb("slots_rstd", [P, B, T])
        vec = sb("vec", [P, C, NV])
        ident = sb("ident", [P, P])
        mean_r = sb("mean_r", [P, P], F32R)
        ones_r = sb("ones_r", [P, P], F32R)
        snew = sb("snew", [P, J, C, BANK])
        order = sb("order", [P, E])
        epsc = sb("epsc", [P, 2])

        consts_in, consts_set = sem("consts_in"), sem("consts_set")
        s_hi, s_lo, sq_done, ssum_done = sem("s_hi"), sem("s_lo"), sem("sq_done"), sem("ssum_done")

        def col(c, i):
            return vec[:, c, i:i + 1]

        def rsqrt_steps(eng, link, v, y, t, eps):
            link(eng.tensor_scalar(v, v, eps, None, ALU.add))
            link(eng.tensor_scalar(t.bitcast(I32), v.bitcast(I32), 1, None, ALU.logical_shift_right))
            link(eng.tensor_scalar(y.bitcast(I32), t.bitcast(I32), -1, RSQRT_SEED, ALU.mult, ALU.add))
            for _ in range(3):
                link(eng.tensor_tensor(t, y, y, ALU.mult))
                link(eng.scalar_tensor_tensor(out=t, in0=t, scalar=-0.5, in1=v, op0=ALU.mult, op1=ALU.mult))
                link(eng.scalar_tensor_tensor(out=y, in0=t, scalar=1.5, in1=y, op0=ALU.add, op1=ALU.mult))
        RSQRT_OPS = 12

        class Chain:

            def __init__(self, eng, s, base):
                self.eng, self.s, self.n = eng, s, base

            def __call__(self, ins):
                ins.then_inc(self.s, 1)
                self.n = self.n + 1
                self.eng.wait_ge(self.s, self.n)

        w1_in, w1_hi, w1_lo = sem("w1_in"), sem("w1_hi"), sem("w1_lo")
        x_in, xt_in, x_hi, x_lo = sem("x_in"), sem("xt_in"), sem("x_hi"), sem("x_lo")
        gate_mm, val_mm, gate_ev, val_ev = sem("gate_mm"), sem("val_mm"), sem("gate_ev"), sem("val_ev")
        tap_act, tap_pool, conv = sem("tap_act"), sem("tap_pool"), sem("conv")
        gated, scanned, y_hi, y_lo = sem("gated"), sem("scanned"), sem("y_hi"), sem("y_lo")
        out_mm, res_done, xb_done = sem("out_mm"), sem("res_done"), sem("xb_done")
        ln_chain, x1_ready, x1_saved = sem("ln_chain"), sem("x1_ready"), sem("x1_saved")
        x1_T, x1_ev = sem("x1_T"), sem("x1_ev")

        p1 = ExitStack()
        sb1 = space(p1)
        xF = sb1("x_fm", [P, C, T])
        xs = [sb1("x_fm_hi", [P, C, T], F32R), sb1("x_fm_lo", [P, C, T], F32R)]
        xt = sb1("x_tm", [P, NT, D])
        g = sb1("g", [P, C, T])
        val = sb1("val", [P, C, T + 2 * HALO])
        cv = sb1("cv", [P, C, T])
        tap = sb1("tap", [P, BANK])
        ys = [sb1("y_fm_hi", [P, C, T], F32R), sb1("y_fm_lo", [P, C, T], F32R)]
        wi = [sb1(f"w_in{i}", [P, C, 2 * D], F32R) for i in range(2)]
        wo = [sb1(f"w_out{i}", [P, C, D], F32R) for i in range(2)]
        lw = sb1("ln_w", [P, D])
        lb = sb1("ln_b", [P, D])
        res = sb1("res", [P, TJ, D])
        x1t = sb1("x1_tm", [P, TJ, D])
        sq = sb1("sq", [P, C, BANK])
        st6 = sb1("st6", [P, TJ, 6])
        mv = sb1("mv", [P, TJ, 2])
        ln2 = sb1("ln2", [P, 2, TJ])
        acol = sb1("acol", [P, C])
        spare = sb1("spare", [P, 1])
        raw_wi = res[:].rearrange("p t d -> p (t d)").rearrange("p (c n) -> p c n", c=C)
        raw_wo = x1t[:, 0:C, :]
        GB, VB, OB, TB = 0, 2, 4, 6
        TAPS = K - 2

        def is_first(b):
            return isinstance(b, int) and b == 0

        def known(k):
            return isinstance(k, int)

        with nc.Block() as block:
            @block.sync
            def _(sp):
                sp.dma_start(xF[:], xT_v[:, :, 0]).then_inc(x_in, 16)
                sp.dma_start(raw_wi, chunks(w_inT)).then_inc(w1_in, 16)
                sp.dma_start(raw_wo, chunks(w_outT)).then_inc(w1_in, 16)
                sp.dma_start(vec[:], vecs).then_inc(consts_in, 16)
                sp.dma_start(ident[:], ident_in).then_inc(consts_in, 16)
                sp.dma_start(order[:], order_in).then_inc(consts_in, 16)
                sp.dma_start(lw[:], lnw.partition_broadcast(P)).then_inc(consts_in, 16)
                sp.dma_start(lb[:], lnb.partition_broadcast(P)).then_inc(consts_in, 16)
                sp.dma_start(xt[:], x_v[:, 0]).then_inc(xt_in, 16)

                def save_block(b, j):
                    sp.wait_ge(x1_ready, J * b + j + 1)
                    sp.dma_start(x1_v[:, b, j * TJ:(j + 1) * TJ], x1t[:]).then_inc(x1_saved, 16)

                def load_fm(b):
                    sp.wait_ge(x_lo, b)
                    sp.dma_start(xF[:], xT_v[:, :, b]).then_inc(x_in, 16)

                def load_tm(b):
                    save_block(b - 1, 0)
                    save_block(b - 1, 1)
                    sp.dma_start(xt[:], x_v[:, b]).then_inc(xt_in, 16)

                load_fm(1)
                with sp.Fori(1, B - 1) as b:
                    load_fm(b + 1)
                    load_tm(b)
                load_tm(B - 1)
                save_block(B - 1, 0)
                save_block(B - 1, 1)
                sp.wait_ge(x1_saved, 16 * J * B)

            @block.scalar
            def _(act):
                def split_x(b):
                    act.wait_ge(x_in, 16 * b + 16)
                    if not is_first(b):
                        act.wait_ge(val_mm, J * C * b)
                    act.activation(xs[0][:], xF[:], ACT.Copy).then_inc(x_hi, 1)

                def values(b):
                    for c in range(C):
                        n = C * b + c
                        if not is_first(b):
                            act.wait_ge(y_lo, n - C + 1)
                            act.wait_ge(conv, TAPS * (n - C + 1))
                        for j in range(J):
                            act.wait_ge(gate_mm, J * n + j + 1)
                            act.activation(g[:, c, j * BANK:(j + 1) * BANK], psum[:, GB + j, :],
                                           ACT.Sigmoid).then_inc(gate_ev, 1)
                        for j in range(J):
                            act.wait_ge(val_mm, J * n + j + 1)
                            act.activation(val[:, c, HALO + j * BANK:HALO + (j + 1) * BANK],
                                           psum[:, VB + j, :], ACT.Copy).then_inc(val_ev, 1)
                        act.wait_ge(val_ev, J * n + J)
                        act.activation(cv[:, c, :], val[:, c, 0:T], ACT.Identity, bias=col(c, V_CB),
                                       scale=col(c, 0)).then_inc(tap_act, 1)
                        for j in range(J):
                            if not (is_first(b) and c == 0 and j == 0):
                                act.wait_ge(tap_pool, J * n + j)
                            act.activation(tap[:], val[:, c, K - 1 + j * BANK:K - 1 + (j + 1) * BANK],
                                           ACT.Copy, scale=col(c, K - 1)).then_inc(tap_act, 1)

                def split_y(b):
                    for c in range(C):
                        act.wait_ge(scanned, C * b + c + 1)
                        if not is_first(b):
                            act.wait_ge(out_mm, NT * b)
                        act.activation(ys[0][:, c, :], g[:, c, :], ACT.Copy).then_inc(y_hi, 1)

                def new_slots(b):
                    for j in range(J):
                        m = J * b + j
                        if not is_first(b):
                            act.wait_ge(s_lo, J * b)
                        for t in range(TJ):
                            i = NT * b + TJ * j + t
                            act.wait_ge(x1_T, i + 1)
                            act.activation(snew[:, j, :, t * P:(t + 1) * P],
                                           psum[:, TB + t % 2, 0:D].rearrange("p (c t) -> p c t", c=C),
                                           ACT.Copy).then_inc(x1_ev, 1)
                        act.wait_ge(x1_ev, NT * b + TJ * (j + 1))
                        act.activation(slots[0][:, :, b, j * BANK:(j + 1) * BANK], snew[:, j, :, :],
                                       ACT.Copy).then_inc(s_hi, 1)
                        if not (is_first(b) and j == 0):
                            act.wait_ge(ssum_done, m)
                        act.activation(sq[:], snew[:, j, :, :], ACT.Square).then_inc(sq_done, 1)

                act.wait_ge(w1_in, 32)
                act.activation(wi[0][:], raw_wi, ACT.Copy).then_inc(w1_hi, 1)
                act.activation(wo[0][:], raw_wo, ACT.Copy).then_inc(w1_hi, 1)
                act.wait_ge(consts_in, 80)
                act.activation(acol[:], vec[:, :, V_A], ACT.Tanh).then_inc(consts_set, 1)
                split_x(0)
                act.wait_ge(consts_set, 7)
                values(0)
                split_x(1)
                split_y(0)

                def step(b):
                    values(b)
                    if not known(b) or b + 1 < B:
                        split_x(b + 1)
                    split_y(b)
                    new_slots(b - 1)

                step(1)
                with act.Fori(2, B - 1) as b:
                    step(b)
                step(B - 1)
                new_slots(B - 1)

            @block.gpsimd
            def _(pool):
                def split_x(b):
                    pool.wait_ge(x_hi, b + 1)
                    pool.tensor_tensor(xs[1][:], xF[:], xs[0][:].bitcast(F32), ALU.subtract).then_inc(x_lo, 1)

                def values(b):
                    for c in range(C):
                        for j in range(J):
                            n = C * b + c
                            pool.wait_ge(tap_act, (J + 1) * n + 2 + j)
                            part = cv[:, c, j * BANK:(j + 1) * BANK]
                            pool.tensor_tensor(part, part, tap[:], ALU.add).then_inc(tap_pool, 1)
                    for c in range(C):
                        pool.wait_ge(conv, TAPS * (C * b + c + 1))
                        pool.tensor_tensor(cv[:, c, :], cv[:, c, :], g[:, c, :], ALU.mult).then_inc(gated, 1)

                def split_y(b):
                    for c in range(C):
                        pool.wait_ge(y_hi, C * b + c + 1)
                        pool.tensor_tensor(ys[1][:, c, :], g[:, c, :], ys[0][:, c, :].bitcast(F32),
                                           ALU.subtract).then_inc(y_lo, 1)

                def add_bias(b):
                    for j in range(J):
                        pool.wait_ge(res_done, NT * b + TJ * (j + 1))
                        part = xt[:, j * TJ:(j + 1) * TJ, :]
                        bias = lb[:].rearrange("p (a d) -> p a d", a=1).broadcast_to([P, TJ, D])
                        pool.tensor_tensor(part, part, bias, ALU.add).then_inc(xb_done, 1)

                def new_slots(b):
                    for j in range(J):
                        m = J * b + j
                        pool.wait_ge(s_hi, m + 1)
                        cols = slice(j * BANK, (j + 1) * BANK)
                        pool.tensor_tensor(slots[1][:, :, b, cols], snew[:, j, :, :],
                                           slots[0][:, :, b, cols].bitcast(F32), ALU.subtract).then_inc(s_lo, 1)
                        pool.wait_ge(sq_done, m + 1)
                        pool.tensor_tensor(rstd[:, b, cols], sq[:, 0, :], sq[:, 1, :],
                                           ALU.add).then_inc(ssum_done, 1)

                pool.memset(mean_r[:].bitcast(F32), 1.0 / D).then_inc(consts_set, 1)
                pool.memset(ones_r[:].bitcast(F32), 1.0).then_inc(consts_set, 1)
                pool.memset(val[:, :, 0:HALO], 0.0).then_inc(consts_set, 1)
                pool.memset(val[:, :, HALO + T:], 0.0).then_inc(consts_set, 1)
                pool.memset(epsc[:, 0:1], EPS_RMS).then_inc(consts_set, 1)
                pool.memset(epsc[:, 1:2], EPS_ATTN).then_inc(consts_set, 1)
                split_x(0)
                values(0)
                split_x(1)
                split_y(0)

                def step(b):
                    values(b)
                    if not known(b) or b + 1 < B:
                        split_x(b + 1)
                    add_bias(b - 1)
                    split_y(b)
                    new_slots(b - 1)

                step(1)
                with pool.Fori(2, B - 1) as b:
                    step(b)
                step(B - 1)
                add_bias(B - 1)
                new_slots(B - 1)

            @block.tensor
            def _(pe):
                def project(b):
                    pe.wait_ge(x_hi, b + 1)
                    pe.wait_ge(x_lo, b + 1)
                    for c in range(C):
                        n = C * b + c
                        for bank, done, free, at in ((GB, gate_mm, gate_ev, c * P), (VB, val_mm, val_ev, D + c * P)):
                            for j in range(J):
                                if not (is_first(b) and c == 0):
                                    pe.wait_ge(free, J * (n - 1) + j + 1)
                                todo = [(k, w, d) for k in range(C) for w, d in PASSES]
                                for i, (k, w, d) in enumerate(todo):
                                    last = pe.matmul(psum[:, bank + j, :], wi[w][:, k, at:at + P],
                                                     xs[d][:, k, j * BANK:(j + 1) * BANK],
                                                     start=i == 0, stop=i == len(todo) - 1)
                                last.then_inc(done, 1)

                def output(b):
                    pe.wait_ge(y_hi, C * b + C)
                    pe.wait_ge(y_lo, C * b + C)
                    for t in range(NT):
                        if not (is_first(b) and t < 2):
                            pe.wait_ge(res_done, NT * b + max(t - 1, 0))
                        todo = [(k, w, d) for k in range(C) for w, d in PASSES]
                        for i, (k, w, d) in enumerate(todo):
                            last = pe.matmul(psum[:, OB + t % 2, 0:D], ys[d][:, k, t * P:(t + 1) * P],
                                             wo[w][:, k, :], start=i == 0, stop=i == len(todo) - 1)
                        last.then_inc(out_mm, 1)
                    for j in range(J):
                        pe.wait_ge(x1_ready, J * b + j + 1)
                        for t in range(TJ):
                            i = TJ * j + t
                            if not (is_first(b) and i < 2):
                                pe.wait_ge(x1_ev, NT * b + max(i - 1, 0))
                            for c in range(C):
                                last = pe.transpose(psum[:, TB + t % 2, c * P:(c + 1) * P],
                                                    x1t[:, t, c * P:(c + 1) * P], ident[:])
                            last.then_inc(x1_T, 1)

                pe.wait_ge(consts_in, 80)
                pe.wait_ge(w1_hi, 2)
                pe.wait_ge(w1_lo, 2)
                project(0)
                project(1)
                output(0)
                with pe.Fori(2, B) as b:
                    project(b)
                    output(b - 1)
                output(B - 1)

            @block.vector
            def _(dve):
                def values(b):
                    for c in range(C):
                        n = C * b + c
                        dve.wait_ge(tap_pool, J * n + J)
                        for i, k in enumerate(range(1, K - 1)):
                            dve.scalar_tensor_tensor(out=cv[:, c, :], in0=val[:, c, k:k + T], scalar=col(c, k),
                                                     in1=cv[:, c, :], op0=ALU.mult, op1=ALU.add).then_inc(conv, 1)
                            if i < TAPS - 1:
                                dve.wait_ge(conv, TAPS * n + i + 1)
                    for c in range(C):
                        n = C * b + c
                        dve.wait_ge(gated, n + 1)
                        dve.tensor_tensor_scan(out=g[:, c, :], data0=acol[:, c:c + 1].broadcast_to([P, T]),
                                               data1=cv[:, c, :], initial=0.0, op0=ALU.mult,
                                               op1=ALU.add).then_inc(scanned, 1)

                def norms(b):
                    dve.wait_ge(xt_in, 16 * b + 16)
                    for j in range(J):
                        m = J * b + j
                        link = Chain(dve, ln_chain, m * (6 + 2 * RSQRT_OPS))

                        def stats():
                            for t in range(TJ):
                                last = dve.bn_stats(st6[:, t, :], res[:, t, :])
                            link(last)
                            dve.memset(spare[:], 0.0)
                            for t in range(TJ):
                                last = dve.bn_aggr(mv[:, t, :], st6[:, t, :])
                            link(last)
                            rsqrt_steps(dve, link, mv[:, :, 1], ln2[:, 0, :], ln2[:, 1, :], EPS_LN)

                        if not (is_first(b) and j == 0):
                            dve.wait_ge(x1_ready, m)
                        for t in range(TJ):
                            i = TJ * j + t
                            dve.wait_ge(out_mm, NT * b + i + 1)
                            dve.tensor_tensor(res[:, t, :], psum[:, OB + t % 2, 0:D], xt[:, i, :],
                                              ALU.add).then_inc(res_done, 1)
                        dve.wait_ge(res_done, NT * b + TJ * (j + 1))
                        stats()
                        for t in range(TJ):
                            last = dve.scalar_tensor_tensor(out=res[:, t, :], in0=res[:, t, :], scalar=mv[:, t, 0:1],
                                                            in1=lw[:], op0=ALU.subtract, op1=ALU.mult)
                        link(last)
                        dve.wait_ge(xb_done, m + 1)
                        for t in range(TJ):
                            last = dve.scalar_tensor_tensor(out=res[:, t, :], in0=res[:, t, :],
                                                            scalar=ln2[:, 0, t:t + 1], in1=xt[:, TJ * j + t, :],
                                                            op0=ALU.mult, op1=ALU.add)
                        link(last)
                        stats()
                        if not (is_first(b) and j == 0):
                            dve.wait_ge(x1_T, TJ * m)
                            dve.wait_ge(x1_saved, 16 * m)
                        for t in range(TJ):
                            last = dve.tensor_scalar(x1t[:, t, :], res[:, t, :], mv[:, t, 0:1],
                                                     ln2[:, 0, t:t + 1], ALU.subtract, ALU.mult)
                        last.then_inc(x1_ready, 1)

                dve.wait_ge(w1_hi, 1)
                dve.tensor_tensor(wi[1][:], raw_wi, wi[0][:].bitcast(F32), ALU.subtract).then_inc(w1_lo, 1)
                dve.wait_ge(w1_hi, 2)
                dve.tensor_tensor(wo[1][:], raw_wo, wo[0][:].bitcast(F32), ALU.subtract).then_inc(w1_lo, 1)
                dve.wait_ge(w1_lo, 2)
                dve.wait_ge(consts_in, 80)
                dve.wait_ge(consts_set, 7)
                values(0)
                values(1)
                norms(0)
                with dve.Fori(2, B) as b:
                    values(b)
                    norms(b - 1)
                norms(B - 1)
        p1.close()


        ctx_in, w2_in = sem("ctx_in"), sem("w2_in")
        ctx_sq, ctx_ms, ctx_ln, ctx_rs, ctx_n = (
            sem("ctx_sq"), sem("ctx_ms"), sem("ctx_ln"), sem("ctx_rs"), sem("ctx_n"))
        k_mm, k_ev, v_mm, v_ev = sem("k_mm"), sem("k_ev"), sem("v_mm"), sem("v_ev")
        fold_mm, fold_ev, fold_hi, fold_lo = sem("fold_mm"), sem("fold_ev"), sem("fold_hi"), sem("fold_lo")
        vp_mm, vp_hi, vp_lo, wh_hi, wh_lo = sem("vp_mm"), sem("vp_hi"), sem("vp_lo"), sem("wh_hi"), sem("wh_lo")
        bias_set = sem("bias_set")

        p2 = ExitStack()
        sb2 = space(p2)
        wh = [sb2(f"w_hh{i}", [P, C, G3], F32R) for i in range(2)]
        fold = [sb2(f"fold{i}", [P, C, B, 2, M], F32R) for i in range(2)]
        vp = [sb2(f"v_ih{i}", [P, B, G3], F32R) for i in range(2)]
        brz = sb2("brz", [P, C, 2])

        prep = ExitStack()
        sb3 = space(prep)
        cx = sb3("cx", [P, C, B * M])
        cn = sb3("cn", [P, C, B * M])
        crs = sb3("crs", [P, B * M])
        kT = sb3("kT", [P, C, B * M])
        vd = sb3("vd", [P, C, B, 2, M])
        fraw = sb3("fraw", [P, C, B * M])
        wq_r, wk_r, wv_r = (sb3(n, [P, C, D]) for n in ("wq_raw", "wk_raw", "wv_raw"))
        wih_r, whh_r = (sb3(n, [P, C, G3]) for n in ("wih_raw", "whh_raw"))
        HG = G3 // 2
        mean_f = mean_r[:].bitcast(F32)

        with nc.Block() as block:
            @block.sync
            def _(sp):
                sp.dma_start(cx[:], chunks(ctxT)).then_inc(ctx_in, 16)
                sp.dma_start(whh_r[:], chunks(whhT)).then_inc(w2_in, 16)
                for w, src in ((wk_r, wkT), (wv_r, wvT), (wq_r, wq), (wih_r, wihT)):
                    sp.dma_start(w[:], chunks(src)).then_inc(ctx_in, 16)

            @block.scalar
            def _(act):
                act.wait_ge(ctx_in, 80)
                act.activation(cn[:], cx[:], ACT.Square).then_inc(ctx_sq, 1)
                act.wait_ge(ctx_ms, 1)
                act.activation(crs[:], psum[:, 0, 0:B * M], ACT.Ln, bias=epsc[:, 0:1]).then_inc(ctx_ln, 1)
                act.wait_ge(ctx_ln, 1)
                act.activation(crs[:], crs[:], ACT.Exp, scale=-0.5).then_inc(ctx_rs, 1)
                for c in range(C):
                    act.wait_ge(k_mm, c + 1)
                    act.activation(kT[:, c, :], psum[:, 1 + c, 0:B * M], ACT.Copy).then_inc(k_ev, 1)
                act.wait_ge(w2_in, 16)
                act.activation(wh[0][:], whh_r[:], ACT.Copy).then_inc(wh_hi, 1)
                for c in range(C):
                    act.wait_ge(fold_ev, c + 1)
                    for h in range(2):
                        act.activation(fold[0][:, c, :, h, :], fraw[:, c, :].rearrange("p (b m) -> p b m", b=B),
                                       ACT.Copy).then_inc(fold_hi, 1)
                for b in range(B):
                    for h in range(2):
                        i = 2 * b + h
                        act.wait_ge(vp_mm, i + 1)
                        act.activation(vp[0][:, b, h * HG:(h + 1) * HG], psum[:, 4 + i % 4, 0:HG],
                                       ACT.Copy).then_inc(vp_hi, 1)

            @block.tensor
            def _(pe):
                pe.wait_ge(ctx_sq, 1)
                for c in range(C):
                    last = pe.matmul(psum[:, 0, 0:B * M], mean_f, cn[:, c, :], start=c == 0, stop=c == C - 1)
                last.then_inc(ctx_ms, 1)
                pe.wait_ge(ctx_n, C)
                for bank, w, done in ((1, wk_r, k_mm), (3, wv_r, v_mm)):
                    for c in range(C):
                        for k in range(C):
                            last = pe.matmul(psum[:, bank + c, 0:B * M], w[:, k, c * P:(c + 1) * P], cn[:, k, :],
                                             start=k == 0, stop=k == C - 1)
                        last.then_inc(done, 1)
                pe.wait_ge(k_ev, C)
                for c in range(C):
                    for k in range(C):
                        last = pe.matmul(psum[:, 1 + c, 0:B * M], wq_r[:, k, c * P:(c + 1) * P], kT[:, k, :],
                                         start=k == 0, stop=k == C - 1)
                    last.then_inc(fold_mm, 1)
                pe.wait_ge(v_ev, 2 * C)
                for b in range(B):
                    for h in range(2):
                        i = 2 * b + h
                        if i >= 4:
                            pe.wait_ge(vp_hi, i - 3)
                            pe.wait_ge(vp_lo, i - 3)
                        for k in range(C):
                            last = pe.matmul(psum[:, 4 + i % 4, 0:HG],
                                             vd[:, k, b].rearrange("p h m -> p (h m)"),
                                             wih_r[:, k, h * HG:(h + 1) * HG], start=k == 0, stop=k == C - 1)
                        last.then_inc(vp_mm, 1)

            @block.vector
            def _(dve):
                for c in range(C):
                    dve.tensor_tensor(brz[:, c, :], vec[:, c, V_BIH:V_BIH + 2], vec[:, c, V_BHH:V_BHH + 2],
                                      ALU.add).then_inc(bias_set, 1)
                dve.wait_ge(ctx_rs, 1)
                for c in range(C):
                    dve.scalar_tensor_tensor(out=cn[:, c, :], in0=cx[:, c, :], scalar=col(c, V_IN), in1=crs[:],
                                             op0=ALU.mult, op1=ALU.mult).then_inc(ctx_n, 1)
                for c in range(C):
                    dve.wait_ge(v_mm, c + 1)
                    for h in range(2):
                        dve.tensor_copy(vd[:, c, :, h, :],
                                        psum[:, 3 + c, 0:B * M].rearrange("p (b m) -> p b m", b=B)).then_inc(v_ev, 1)
                for c in range(C):
                    dve.wait_ge(fold_mm, c + 1)
                    dve.tensor_scalar(fraw[:, c, :], psum[:, 1 + c, 0:B * M], col(c, V_SN), SCALE,
                                      ALU.mult, ALU.mult).then_inc(fold_ev, 1)
                dve.wait_ge(wh_hi, 1)
                dve.tensor_tensor(wh[1][:], whh_r[:], wh[0][:].bitcast(F32), ALU.subtract).then_inc(wh_lo, 1)
                for c in range(C):
                    for h in range(2):
                        dve.wait_ge(fold_hi, 2 * c + h + 1)
                        dve.tensor_tensor(fold[1][:, c, :, h, :], fraw[:, c, :].rearrange("p (b m) -> p b m", b=B),
                                          fold[0][:, c, :, h, :].bitcast(F32), ALU.subtract).then_inc(fold_lo, 1)
                for b in range(B):
                    for h in range(2):
                        i = 2 * b + h
                        part = slice(h * HG, (h + 1) * HG)
                        dve.wait_ge(vp_hi, i + 1)
                        dve.tensor_tensor(vp[1][:, b, part], psum[:, 4 + i % 4, 0:HG],
                                          vp[0][:, b, part].bitcast(F32), ALU.subtract).then_inc(vp_lo, 1)
        prep.close()

        score_mm, scaled, topped, exped, inverted = (
            sem("score_mm"), sem("scaled"), sem("topped"), sem("exped"), sem("inverted"))
        stack_hi, stack_lo, d_mm, d_ln, d_rd = sem("stack_hi"), sem("stack_lo"), sem("d_mm"), sem("d_ln"), sem("d_rd")
        attn_done, at_hi, at_lo = sem("attn_done"), sem("at_hi"), sem("at_lo")
        r_mm, hn_mm, xn_mm, z_mm = sem("r_mm"), sem("hn_mm"), sem("xn_mm"), sem("z_mm")
        r_act, z_act, n_act, t_dve, t2_dve = sem("r_act"), sem("z_act"), sem("n_act"), sem("t_dve"), sem("t2_dve")
        d_pool, e_dve, s_dve = sem("d_pool"), sem("e_dve"), sem("s_dve")
        ss_hi, ss_lo, ss_mm, ss_ln, rstd_done = (
            sem("ss_hi"), sem("ss_lo"), sem("ss_mm"), sem("ss_ln"), sem("rstd_done"))

        tmp = ExitStack()
        sb4 = space(tmp)
        rb, tb, nb, zb, db = (sb4(n, [P, C, BANK]) for n in ("rb", "tb", "nb", "zb", "db"))
        sc = sb4("sc", [P, T])
        stack = sb4("stack", [P, T], F32R)
        rd = sb4("rd", [P, T])
        an = sb4("an", [P, T])
        at = [sb4(f"at{i}", [P, T], F32R) for i in range(2)]
        ssp = [sb4("ss_hi_t", [P, T], F32R), sb4("ss_lo_t", [P, T], F32R)]
        sq2 = sb4("sq2", [P, J, C, BANK])
        small = sb4("small", [P, 4])
        LOW = slice(M, P)
        R_B, HN_B, XN_B, Z_B, S_B, Q_B = 0, 1, 2, 3, 4, 6

        def blk(j):
            return slice(j * BANK, (j + 1) * BANK)

        with nc.Block() as block:
            @block.tensor
            def _(pe):
                def scores(k, b):
                    pe.wait_ge(s_hi, J * k + J)
                    pe.wait_ge(s_lo, J * k + J)
                    if not (known(k) and k == 0):
                        pe.wait_ge(d_ln, k)
                    for j in range(J):
                        todo = [(c, w, d) for c in range(C) for w, d in PASSES]
                        for i, (c, w, d) in enumerate(todo):
                            last = pe.matmul(psum[:, S_B + j, :], fold[w][:, c, b].rearrange("p h m -> p (h m)"),
                                             slots[d][:, c, b, blk(j)], start=i == 0, stop=i == len(todo) - 1)
                        last.then_inc(score_mm, 1)

                def sums(k):
                    pe.wait_ge(stack_lo, k + 1)
                    for j in range(J):
                        last = pe.matmul(psum[:, S_B + j, :], ones_r[:], stack[:, blk(j)], start=True, stop=True)
                    last.then_inc(d_mm, 1)

                def mean_squares(f):
                    pe.wait_ge(ss_lo, f + 1)
                    if not (known(f) and f == 0):
                        pe.wait_ge(ss_ln, f)
                    for j in range(J):
                        for d in range(2):
                            last = pe.matmul(psum[:, Q_B + j, :], mean_r[:], ssp[d][:, blk(j)],
                                             start=d == 0, stop=d == 1)
                    last.then_inc(ss_mm, 1)

                def unit(k, b, q):
                    j, c = q // C, q % C
                    u = U * k + q
                    first = known(k) and k == 0 and q == 0

                    def hidden(gate):
                        return [(wh[w][:, i, gate * D + c * P:gate * D + (c + 1) * P], slots[d][:, i, b, blk(j)])
                                for i in range(C) for w, d in PASSES]

                    def update(gate):
                        return [(vp[w][:, b, gate * D + c * P:gate * D + (c + 1) * P], at[b % 2][:, blk(j)])
                                for w in range(2)]

                    def run(bank, pairs, done, start=True, stop=True):
                        for i, (w, d) in enumerate(pairs):
                            last = pe.matmul(psum[:, bank, :], w, d, start=start and i == 0,
                                             stop=stop and i == len(pairs) - 1)
                        if stop:
                            last.then_inc(done, 1)

                    if not first:
                        pe.wait_ge(r_act, u)
                    run(R_B, hidden(0), r_mm, stop=False)
                    if q == 0:
                        pe.wait_ge(at_lo, k + 1)
                    run(R_B, update(0), r_mm, start=False)
                    if not first:
                        pe.wait_ge(t_dve, u)
                    run(HN_B, hidden(2), hn_mm)
                    if not first:
                        pe.wait_ge(t2_dve, u)
                    run(XN_B, update(2), xn_mm)
                    if not first:
                        pe.wait_ge(z_act, u)
                    run(Z_B, hidden(1) + update(1), z_mm)

                def step(k, b):
                    if not known(k) or k + 1 < STEPS:
                        scores(k + 1, (b + 1) % B)
                    unit(k, b, 0)
                    unit(k, b, 1)
                    if not known(k) or k + 1 < STEPS:
                        sums(k + 1)
                    unit(k, b, 2)
                    if not known(k) or k + 3 < STEPS:
                        mean_squares(k + 3)
                    unit(k, b, 3)

                pe.wait_ge(wh_lo, 1)
                pe.wait_ge(fold_lo, 2 * C)
                pe.wait_ge(vp_lo, 2 * B)
                for f in range(3):
                    mean_squares(f)
                scores(0, 0)
                sums(0)
                for b in range(B):
                    step(b, b)
                with pe.Fori(1, ITERS - 1) as it:
                    for b in range(B):
                        step(B * it + b, b)
                for b in range(B):
                    step(B * (ITERS - 1) + b, b)

            @block.scalar
            def _(act):
                def split_sums(f, b):
                    act.wait_ge(ssum_done, J * f + J)
                    if not (known(f) and f == 0):
                        act.wait_ge(ss_mm, f)
                    act.activation(ssp[0][:], rstd[:, b, :], ACT.Copy).then_inc(ss_hi, 1)

                def rms(f, b):
                    act.wait_ge(ss_mm, f + 1)
                    act.activation(rstd[:, b, :].rearrange("p (j n) -> p j n", j=J), psum[:, Q_B:Q_B + J, :], ACT.Ln,
                                   bias=epsc[:, 0:1]).then_inc(ss_ln, 1)
                    act.wait_ge(ss_ln, f + 1)
                    act.activation(rstd[:, b, :], rstd[:, b, :], ACT.Exp, scale=-0.5).then_inc(rstd_done, 1)

                def exponentials(k):
                    act.wait_ge(topped, 2 * k + 2)
                    act.activation(sc[:], sc[:], ACT.Exp, bias=small[:, 1:2],
                                   accum_out=small[:, 2:3]).then_inc(exped, 1)

                def normaliser(k):
                    act.wait_ge(d_mm, k + 1)
                    act.activation(rd[:].rearrange("p (j n) -> p j n", j=J), psum[:, S_B:S_B + J, :], ACT.Ln,
                                   bias=epsc[:, 1:2]).then_inc(d_ln, 1)
                    act.wait_ge(d_ln, k + 1)
                    act.activation(rd[:], rd[:], ACT.Exp, scale=-1.0).then_inc(d_rd, 1)

                def attention_hi(k, b):
                    act.wait_ge(attn_done, k + 1)
                    act.activation(at[b % 2][:], an[:], ACT.Copy).then_inc(at_hi, 1)

                def r_gate(k, q):
                    c = q % C
                    act.wait_ge(r_mm, U * k + q + 1)
                    act.activation(rb[:, c, :], psum[:, R_B, :], ACT.Sigmoid, bias=brz[:, c, 0:1]).then_inc(r_act, 1)

                def nz_gates(k, q):
                    c, u = q % C, U * k + q
                    act.wait_ge(t2_dve, u + 1)
                    act.activation(nb[:, c, :], tb[:, c, :], ACT.Tanh, bias=col(c, V_BIH + 2)).then_inc(n_act, 1)
                    act.wait_ge(z_mm, u + 1)
                    act.activation(zb[:, c, :], psum[:, Z_B, :], ACT.Sigmoid, bias=brz[:, c, 1:2]).then_inc(z_act, 1)

                def finish(k, b, j):
                    act.wait_ge(s_dve, U * k + C * (j + 1))
                    act.activation(slots[0][:, :, b, blk(j)], snew[:, j, :, :], ACT.Copy).then_inc(s_hi, 1)
                    if not known(k) or k + B < STEPS:
                        act.activation(sq2[:, j, :, :], snew[:, j, :, :], ACT.Square).then_inc(sq_done, 1)

                def step(k, b):
                    last = known(k) and k + 1 >= STEPS
                    r_gate(k, 0)
                    if not last:
                        exponentials(k + 1)
                    if not known(k) or k + 2 < STEPS:
                        rms(k + 2, (b + 2) % B)
                    nz_gates(k, 0)
                    if not known(k) or k + 3 < STEPS:
                        split_sums(k + 3, (b + 3) % B)
                    r_gate(k, 1)
                    nz_gates(k, 1)
                    if not last:
                        normaliser(k + 1)
                    r_gate(k, 2)
                    if not last:
                        attention_hi(k + 1, b + 1)
                    nz_gates(k, 2)
                    r_gate(k, 3)
                    finish(k, b, 0)
                    nz_gates(k, 3)
                    finish(k, b, 1)

                act.wait_ge(bias_set, C)
                split_sums(0, 0)
                for f in range(2):
                    rms(f, f)
                    split_sums(f + 1, f + 1)
                exponentials(0)
                normaliser(0)
                attention_hi(0, 0)
                for b in range(B):
                    step(b, b)
                with act.Fori(1, ITERS - 1) as it:
                    for b in range(B):
                        step(B * it + b, b)
                for b in range(B):
                    step(B * (ITERS - 1) + b, b)

            @block.gpsimd
            def _(pool):
                def difference(k, b, q):
                    j, c = q // C, q % C
                    u = U * k + q
                    pool.wait_ge(n_act, u + 1)
                    pool.tensor_tensor(db[:, c, :], slots[0][:, c, b, blk(j)].bitcast(F32), nb[:, c, :],
                                       ALU.subtract).then_inc(d_pool, 1)
                    pool.wait_ge(d_pool, 2 * u + 1)
                    pool.tensor_tensor(db[:, c, :], db[:, c, :], slots[1][:, c, b, blk(j)].bitcast(F32),
                                       ALU.add).then_inc(d_pool, 1)

                def finish(k, b, j):
                    m = J * (k + B) + j
                    pool.wait_ge(s_hi, m + 1)
                    pool.tensor_tensor(slots[1][:, :, b, blk(j)], snew[:, j, :, :],
                                       slots[0][:, :, b, blk(j)].bitcast(F32), ALU.subtract).then_inc(s_lo, 1)
                    if not known(k) or k + B < STEPS:
                        pool.wait_ge(sq_done, m + 1)
                        pool.tensor_tensor(rstd[:, b, blk(j)], sq2[:, j, 0, :], sq2[:, j, 1, :],
                                           ALU.add).then_inc(ssum_done, 1)

                def step(k, b):
                    for q in range(U):
                        difference(k, b, q)
                    for j in range(J):
                        finish(k, b, j)

                for b in range(B):
                    step(b, b)
                with pool.Fori(1, ITERS - 1) as it:
                    for b in range(B):
                        step(B * it + b, b)
                for b in range(B):
                    step(B * (ITERS - 1) + b, b)

            @block.vector
            def _(dve):
                def split_sums(f, b):
                    dve.wait_ge(ss_hi, f + 1)
                    dve.tensor_tensor(ssp[1][:], rstd[:, b, :], ssp[0][:].bitcast(F32), ALU.subtract).then_inc(ss_lo, 1)

                def tops(k, b):
                    dve.wait_ge(rstd_done, k + 1)
                    for j in range(J):
                        dve.wait_ge(score_mm, J * k + j + 1)
                        dve.tensor_tensor(sc[:, blk(j)], psum[:, S_B + j, :], rstd[:, b, blk(j)],
                                          ALU.mult).then_inc(scaled, 1)
                    dve.wait_ge(scaled, J * k + J)
                    dve.reduce_max(small[:, 0:1], sc[:], AX_X).then_inc(topped, 1)
                    dve.wait_ge(topped, 2 * k + 1)
                    dve.tensor_scalar(small[:, 1:2], small[:, 0:1], -1.0, None, ALU.mult).then_inc(topped, 1)

                def weights(k):
                    dve.wait_ge(exped, k + 1)
                    dve.reciprocal(small[:, 3:4], small[:, 2:3]).then_inc(inverted, 1)
                    dve.wait_ge(inverted, k + 1)
                    dve.tensor_scalar(stack[:], sc[:], small[:, 3:4], None, ALU.mult).then_inc(stack_hi, 1)
                    dve.wait_ge(stack_hi, k + 1)
                    dve.scalar_tensor_tensor(out=stack[LOW, :], in0=sc[LOW, :], scalar=small[LOW, 3:4],
                                             in1=stack[LOW, :].bitcast(F32), op0=ALU.mult,
                                             op1=ALU.subtract).then_inc(stack_lo, 1)

                def attention(k):
                    dve.wait_ge(d_rd, k + 1)
                    dve.scalar_tensor_tensor(out=an[:], in0=sc[:], scalar=small[:, 3:4], in1=rd[:],
                                             op0=ALU.mult, op1=ALU.mult).then_inc(attn_done, 1)

                def attention_lo(k, b):
                    a = at[b % 2]
                    dve.wait_ge(at_hi, k + 1)
                    dve.tensor_tensor(a[LOW, :], an[LOW, :], a[LOW, :].bitcast(F32), ALU.subtract).then_inc(at_lo, 1)

                def candidate(k, q):
                    c, u = q % C, U * k + q
                    dve.wait_ge(r_act, u + 1)
                    dve.wait_ge(hn_mm, u + 1)
                    dve.scalar_tensor_tensor(out=tb[:, c, :], in0=psum[:, HN_B, :], scalar=col(c, V_BHH + 2),
                                             in1=rb[:, c, :], op0=ALU.add, op1=ALU.mult).then_inc(t_dve, 1)
                    dve.wait_ge(t_dve, u + 1)
                    dve.wait_ge(xn_mm, u + 1)
                    dve.tensor_tensor(tb[:, c, :], psum[:, XN_B, :], tb[:, c, :], ALU.add).then_inc(t2_dve, 1)

                def mix(k, q):
                    j, c, u = q // C, q % C, U * k + q
                    dve.wait_ge(z_act, u + 1)
                    dve.wait_ge(d_pool, 2 * u + 2)
                    dve.tensor_tensor(zb[:, c, :], zb[:, c, :], db[:, c, :], ALU.mult).then_inc(e_dve, 1)
                    dve.wait_ge(e_dve, u + 1)
                    dve.tensor_tensor(snew[:, j, c, :], nb[:, c, :], zb[:, c, :], ALU.add).then_inc(s_dve, 1)

                def step(k, b):
                    last = known(k) and k + 1 >= STEPS
                    if not last:
                        tops(k + 1, (b + 1) % B)
                    candidate(k, 0)
                    if not last:
                        weights(k + 1)
                    mix(k, 0)
                    if not known(k) or k + 3 < STEPS:
                        split_sums(k + 3, (b + 3) % B)
                    candidate(k, 1)
                    mix(k, 1)
                    if not last:
                        attention(k + 1)
                    candidate(k, 2)
                    if not last:
                        attention_lo(k + 1, b + 1)
                    mix(k, 2)
                    candidate(k, 3)
                    mix(k, 3)

                for f in range(3):
                    split_sums(f, f)
                tops(0, 0)
                weights(0)
                attention(0)
                attention_lo(0, 0)
                for b in range(B):
                    step(b, b)
                with dve.Fori(1, ITERS - 1) as it:
                    for b in range(B):
                        step(B * it + b, b)
                for b in range(B):
                    step(B * (ITERS - 1) + b, b)
        tmp.close()
        p2.close()

        w3_in, w3_hi, w3_lo = sem("w3_in"), sem("w3_hi"), sem("w3_lo")
        x1_in3 = [sem(f"x1_in3_{j}") for j in range(J)]
        u_done, u_T, w_done, front_chain, back_chain, x2_done = (
            sem("u_done"), sem("u_T"), sem("w_done"), sem("front_chain"), sem("back_chain"),
            sem("x2_done"))
        x2_T, x2_hi, x2_lo, g_mm, route, e_mm = (
            sem("x2_T"), sem("x2_hi"), sem("x2_lo"), sem("g_mm"), sem("route"), sem("e_mm"))
        acc, out_ready = sem("acc"), sem("out_ready")
        out_saved = [sem(f"out_saved_{j}") for j in range(J)]

        p3 = ExitStack()
        sb5 = space(p3)
        ew = [sb5(f"w_expert{i}", [P, C, E * D], F32R) for i in range(2)]
        gw = [sb5(f"w_gate{i}", [P, C, E], F32R) for i in range(2)]
        ew_raw = sb5("w_expert_raw", [P, C, E * D])
        gw_raw = sb5("w_gate_raw", [P, C, E])
        x1g = sb5("x1_group", [P, 2, TJ, D])
        ub = sb5("slots_group", [P, 2, C, BANK])
        wg = sb5("residual_group", [P, TJ, D])
        x2g = sb5("x2_group", [P, 2, TJ, D])
        x2s = [sb5(f"x2_fm{i}", [P, 2, C, P], F32R) for i in range(2)]
        yg = sb5("y_group", [P, TJ, D])
        og = sb5("out_group", [P, 2, TJ, D])
        st3 = sb5("st3", [P, TJ, 6])
        mv3 = sb5("mv3", [P, TJ, 2])
        ln3 = sb5("ln3", [P, 2, TJ])
        sel = sb5("sel", [P, 2, 2, E])
        mx = sb5("mx", [P, 2, 2])
        spare3 = sb5("spare3", [P, 1])
        EP = E * D // BANK
        LN3_OPS = 2 + RSQRT_OPS
        T1, T2, EB = 0, 2, 4


        def group(b, j):
            if j + 1 < J:
                return b, j + 1
            return None if known(b) and b + 1 == B else (b + 1, 0)

        def nexttile(b, j, t):
            if t + 1 < TJ:
                return b, j, t + 1
            g_ = group(b, j)
            return g_ and (*g_, 0)

        def per_sequence(eng, step):
            step(0)
            with eng.Fori(1, B - 1) as b:
                step(b)
            step(B - 1)

        with nc.Block() as block:
            @block.sync
            def _(sp):
                def load(b, j):
                    sp.dma_start(x1g[:, j], x1_v[:, b, j * TJ:(j + 1) * TJ]).then_inc(x1_in3[j], 16)

                load(0, 0)
                load(0, 1)
                sp.dma_start(gw_raw[:], chunks(gateT)).then_inc(w3_in, 16)
                sp.dma_start(ew_raw[:], chunks(expertT)).then_inc(w3_in, 16)

                def step(b):
                    for j in range(J):
                        i = J * b + j
                        if b + 1 < B:
                            sp.wait_ge(w_done, TJ * (i + 1))
                            load(b + 1, j)
                        sp.wait_ge(out_ready, i + 1)
                        sp.dma_start(out_v[:, b, j * TJ:(j + 1) * TJ], og[:, j]).then_inc(out_saved[j], 16)

                for b in range(B):
                    step(b)
                for j in range(J):
                    sp.wait_ge(out_saved[j], 16 * B)

            @block.gpsimd
            def _(pool):
                def step(b):
                    for j in range(J):
                        i = J * b + j
                        if not (known(b) and b == 0):
                            pool.wait_ge(u_T, TJ * (i - 1))
                        pool.tensor_tensor(ub[:, j], slots[0][:, :, b, blk(j)].bitcast(F32),
                                           slots[1][:, :, b, blk(j)].bitcast(F32), ALU.add).then_inc(u_done, 1)

                per_sequence(pool, step)

            @block.scalar
            def _(act):
                def split(b, j, t):
                    n = TJ * (J * b + j) + t
                    act.wait_ge(x2_T, n + 1)
                    if not (known(n) and n < 2):
                        act.wait_ge(e_mm, EP * (n - 1))
                    act.activation(x2s[0][:, t % 2], psum[:, T2 + t % 2, 0:D].rearrange("p (c t) -> p c t", c=C),
                                   ACT.Copy).then_inc(x2_hi, 1)

                act.wait_ge(w3_in, 32)
                act.activation(gw[0][:], gw_raw[:], ACT.Copy).then_inc(w3_hi, 1)
                act.activation(ew[0][:], ew_raw[:], ACT.Copy).then_inc(w3_hi, 1)
                split(0, 0, 0)

                def step(b):
                    for j in range(J):
                        for t in range(TJ):
                            nxt = nexttile(b, j, t)
                            if nxt:
                                split(*nxt)

                per_sequence(act, step)

            @block.tensor
            def _(pe):
                def slots_T(b, j, t):
                    i = J * b + j
                    n = TJ * i + t
                    if t == 0:
                        pe.wait_ge(u_done, i + 1)
                    if not (known(n) and n < 2):
                        pe.wait_ge(w_done, n - 1)
                    for c in range(C):
                        last = pe.transpose(psum[:, T1 + t % 2, c * P:(c + 1) * P], ub[:, j, c, t * P:(t + 1) * P],
                                            ident[:])
                    last.then_inc(u_T, 1)

                def x2_transpose(b, j, t):
                    i = J * b + j
                    n = TJ * i + t
                    if t == 0:
                        pe.wait_ge(x2_done, i + 1)
                    if not (known(n) and n < 2):
                        pe.wait_ge(x2_lo, n - 1)
                        pe.wait_ge(route, 4 * (n - 1))
                    for c in range(C):
                        last = pe.transpose(psum[:, T2 + t % 2, c * P:(c + 1) * P], x2g[:, j, t, c * P:(c + 1) * P],
                                            ident[:])
                    last.then_inc(x2_T, 1)

                def gate(b, j, t):
                    n = TJ * (J * b + j) + t
                    pe.wait_ge(x2_lo, n + 1)
                    todo = [(c, w, d) for c in range(C) for w, d in PASSES]
                    for i, (c, w, d) in enumerate(todo):
                        last = pe.matmul(psum[:, T2 + t % 2, D:D + E], x2s[d][:, t % 2, c, :], gw[w][:, c, :],
                                         start=i == 0, stop=i == len(todo) - 1)
                    last.then_inc(g_mm, 1)

                def expert(b, j, t, pairs):
                    n = TJ * (J * b + j) + t
                    for p in pairs:
                        if not (known(n) and n == 0):
                            pe.wait_ge(acc, E * (n - 1) + 2 * p + 2)
                        todo = [(c, w, d) for c in range(C) for w, d in PASSES]
                        for i, (c, w, d) in enumerate(todo):
                            last = pe.matmul(psum[:, EB + p, :], x2s[d][:, t % 2, c, :],
                                             ew[w][:, c, p * BANK:(p + 1) * BANK], start=i == 0,
                                             stop=i == len(todo) - 1)
                        last.then_inc(e_mm, 1)

                pe.wait_ge(w3_lo, 2)
                for t in range(TJ):
                    slots_T(0, 0, t)
                x2_transpose(0, 0, 0)
                gate(0, 0, 0)

                def step(b):
                    for j in range(J):
                        nxt = group(b, j)
                        for t in range(TJ):
                            if nxt and t < 2:
                                slots_T(*nxt, 2 * t)
                                slots_T(*nxt, 2 * t + 1)
                            tile = nexttile(b, j, t)
                            if tile:
                                x2_transpose(*tile)
                            expert(b, j, t, range(EP // 2))
                            if tile:
                                gate(*tile)
                            expert(b, j, t, range(EP // 2, EP))

                per_sequence(pe, step)

            @block.vector
            def _(dve):
                def residual(b, j, t):
                    i = J * b + j
                    n = TJ * i + t
                    if t == 0:
                        dve.wait_ge(x1_in3[j], 16 * b + 16)
                        if not (known(i) and i == 0):
                            dve.wait_ge(x2_done, i)
                    dve.wait_ge(u_T, n + 1)
                    dve.tensor_tensor(wg[:, t, :], psum[:, T1 + t % 2, 0:D], x1g[:, j, t, :],
                                      ALU.add).then_inc(w_done, 1)

                def statistics(link, src):
                    for t in range(TJ):
                        last = dve.bn_stats(st3[:, t, :], src[:, t, :])
                    link(last)
                    dve.memset(spare3[:], 0.0)
                    for t in range(TJ):
                        last = dve.bn_aggr(mv3[:, t, :], st3[:, t, :])
                    link(last)
                    rsqrt_steps(dve, link, mv3[:, :, 1], ln3[:, 0, :], ln3[:, 1, :], EPS_LN)

                def front_statistics(b, j):
                    i = J * b + j
                    dve.wait_ge(w_done, TJ * i + TJ)
                    statistics(Chain(dve, front_chain, LN3_OPS * i), wg)

                def front_x2(b, j):
                    i = J * b + j
                    for t in range(TJ):
                        last = dve.tensor_scalar(x2g[:, j, t, :], wg[:, t, :], mv3[:, t, 0:1], ln3[:, 0, t:t + 1],
                                                 ALU.subtract, ALU.mult)
                    last.then_inc(x2_done, 1)

                def split(b, j, t):
                    n = TJ * (J * b + j) + t
                    dve.wait_ge(x2_hi, n + 1)
                    dve.tensor_tensor(x2s[1][:, t % 2], psum[:, T2 + t % 2, 0:D].rearrange("p (c t) -> p c t", c=C),
                                      x2s[0][:, t % 2].bitcast(F32), ALU.subtract).then_inc(x2_lo, 1)

                def choose(b, j, t):
                    n = TJ * (J * b + j) + t
                    link = Chain(dve, route, 4 * n)
                    s, v = sel[:, t % 2], mx[:, t % 2]
                    scores = psum[:, T2 + t % 2, D:D + E]
                    dve.wait_ge(g_mm, n + 1)
                    link(dve.reduce_max(v[:, 0:1], scores, AX_X))
                    link(dve.scalar_tensor_tensor(out=s[:, 0, :], in0=scores, scalar=v[:, 0:1], in1=order[:],
                                                  op0=ALU.is_ge, op1=ALU.mult))
                    link(dve.reduce_max(v[:, 1:2], s[:, 0, :], AX_X))
                    link(dve.tensor_scalar(s[:, 1, :], s[:, 0, :], v[:, 1:2], None, ALU.is_equal))

                def combine(b, j, t, experts):
                    n = TJ * (J * b + j) + t
                    if t == 0 and 0 in experts and not (known(n) and n == 0):
                        dve.wait_ge(out_ready, J * b + j)
                    for e in experts:
                        dve.wait_ge(e_mm, EP * n + e // 2 + 1)
                        if e:
                            dve.wait_ge(acc, E * n + e)
                        dve.scalar_tensor_tensor(
                            out=yg[:, t, :], in0=psum[:, EB + e // 2, (e % 2) * D:(e % 2 + 1) * D],
                            scalar=sel[:, t % 2, 1, e:e + 1], in1=yg[:, t, :] if e else x2g[:, j, t, :],
                            op0=ALU.mult, op1=ALU.add).then_inc(acc, 1)

                def back(b, j):
                    i = J * b + j
                    dve.wait_ge(acc, E * TJ * (i + 1))
                    statistics(Chain(dve, back_chain, LN3_OPS * i), yg)
                    if not (known(b) and b == 0):
                        dve.wait_ge(out_saved[j], 16 * b)
                    for t in range(TJ):
                        last = dve.tensor_scalar(og[:, j, t, :], yg[:, t, :], mv3[:, t, 0:1], ln3[:, 0, t:t + 1],
                                                 ALU.subtract, ALU.mult)
                    last.then_inc(out_ready, 1)

                dve.wait_ge(w3_hi, 1)
                dve.tensor_tensor(gw[1][:], gw_raw[:], gw[0][:].bitcast(F32), ALU.subtract).then_inc(w3_lo, 1)
                dve.wait_ge(w3_hi, 2)
                dve.tensor_tensor(ew[1][:], ew_raw[:], ew[0][:].bitcast(F32), ALU.subtract).then_inc(w3_lo, 1)
                for t in range(TJ):
                    residual(0, 0, t)
                front_statistics(0, 0)
                front_x2(0, 0)
                split(0, 0, 0)
                choose(0, 0, 0)

                def step(b):
                    for j in range(J):
                        nxt = group(b, j)
                        for t in range(TJ):
                            if nxt and t < 2:
                                residual(*nxt, 2 * t)
                                residual(*nxt, 2 * t + 1)
                            if nxt and t == 2:
                                front_statistics(*nxt)
                                front_x2(*nxt)
                            tile = nexttile(b, j, t)
                            if tile:
                                split(*tile)
                            combine(b, j, t, range(E // 2))
                            if tile:
                                choose(*tile)
                            combine(b, j, t, range(E // 2, E))
                        back(b, j)

                per_sequence(dve, step)
        p3.close()


_NAMES = ['x', 'xT', 'ctxT', 'vecs', 'w_inT', 'w_outT', 'wq', 'wkT', 'wvT', 'wihT', 'whhT', 'gateT', 'expertT',
          'lnw', 'lnb', 'ident', 'order']


def kernel(x, ctx_1024, L0_attn_W_in, L0_attn_conv_w, L0_attn_conv_b, L0_attn_a_param, L0_attn_W_out, L0_attn_ln_w,
           L0_attn_ln_b, L0_xattn_Wq, L0_xattn_Wk, L0_xattn_Wv, L0_xattn_gru_wih, L0_xattn_gru_whh,
           L0_xattn_gru_bih, L0_xattn_gru_bhh, L0_xattn_slot_norm_w, L0_xattn_input_norm_w, L0_ffn_gate_w,
           L0_ffn_expert_w):
    import numpy as np
    import concourse.bacc as bacc
    from concourse import mybir
    from concourse.bass_utils import run_bass_kernel_spmd

    x_, ctx_ = np.asarray(x), np.asarray(ctx_1024)
    d = x_.shape[-1]
    rows = x_.reshape(-1, d)
    vecs = np.concatenate(
        [np.asarray(L0_attn_conv_w).reshape(d, -1)]
        + [np.asarray(v).reshape(-1, d).T for v in (L0_attn_conv_b, L0_attn_a_param, L0_xattn_slot_norm_w,
                                                    L0_xattn_input_norm_w, L0_xattn_gru_bih, L0_xattn_gru_bhh)],
        axis=1).reshape(2, 128, -1).transpose(1, 0, 2)
    experts = np.asarray(L0_ffn_expert_w)
    n_exp = experts.shape[0]
    arrays = {
        'x': rows, 'xT': rows.T, 'ctxT': ctx_.reshape(-1, d).T, 'vecs': vecs,
        'w_inT': np.asarray(L0_attn_W_in).T, 'w_outT': np.asarray(L0_attn_W_out).T,
        'wq': np.asarray(L0_xattn_Wq), 'wkT': np.asarray(L0_xattn_Wk).T, 'wvT': np.asarray(L0_xattn_Wv).T,
        'wihT': np.asarray(L0_xattn_gru_wih).T, 'whhT': np.asarray(L0_xattn_gru_whh).T,
        'gateT': np.asarray(L0_ffn_gate_w).T,
        'expertT': experts.transpose(2, 0, 1).reshape(d, -1),
        'lnw': np.asarray(L0_attn_ln_w), 'lnb': np.asarray(L0_attn_ln_b),
        'ident': np.eye(128, dtype=np.float32),
        'order': np.tile(np.arange(n_exp, 0, -1, dtype=np.float32), (128, 1)),
    }
    nc = bacc.Bacc("TRN2", target_bir_lowering=False, num_devices=1)
    maps, args = {}, []
    for name in _NAMES:
        a = np.ascontiguousarray(arrays[name])
        maps[f"in_{name}"] = a
        args.append(nc.dram_tensor(f"in_{name}", a.shape, mybir.dt.from_np(a.dtype), kind="ExternalInput").ap())
    out = nc.dram_tensor("out_0", rows.shape, mybir.dt.float32, kind="ExternalOutput").ap()
    x1 = nc.dram_tensor("x1_scratch", rows.shape, mybir.dt.float32, kind="Internal").ap()
    decoder_layer(nc, *args, out, x1)
    r = run_bass_kernel_spmd(nc, [maps], core_ids=[0])
    return r.results[0]["out_0"].reshape(x_.shape)
```
